# Optimizing a Trainium2 kernel written in Bass

```python
import numpy as np
import jax
import jax.numpy as jnp

def _softmax(x, axis=-1):
    return jax.nn.softmax(x, axis=axis)

def _gelu(x):
    return jax.nn.gelu(x, approximate=True)

def _silu(x):
    return jax.nn.silu(x)

def _sigmoid(x):
    return jax.nn.sigmoid(x)

def _layernorm(x, axis=-1, eps=1e-05):
    m = jnp.mean(x, axis=axis, keepdims=True)
    v = jnp.var(x, axis=axis, keepdims=True)
    return (x - m) / jnp.sqrt(v + eps)

def _scatter_add(tgt, idx, src, axis=0):
    return tgt.at[idx].add(src)

def _segment_sum(src, seg, n):
    return jax.ops.segment_sum(src, seg, n)
kernel_name = 'mk_flamingo_gated_d1_seqx_r4_943894'

def setup_inputs(seed: int=0):
    np.random.seed(seed)
    _w = jnp.asarray

    def _rec_inputs():
        import jax
        import jax.numpy as jnp
        _rk = jax.random.key(seed)
        x = -0.000125 + 0.9999 * jax.random.normal(jax.random.fold_in(_rk, 1), (32, 100, 512), jnp.float32)
        _lenS = 100 - jax.random.randint(jax.random.fold_in(_rk, 7), (32,), 0, max(1, 100 // 4) + 1, jnp.int32)
        _lenS2 = 361 - jax.random.randint(jax.random.fold_in(_rk, 8), (32,), 0, max(1, 361 // 4) + 1, jnp.int32)
        _ctx_2048P = jax.random.normal(jax.random.fold_in(_rk, 11), (32, 16, 512), jnp.float32)
        _ctx_2048c = jax.random.dirichlet(jax.random.fold_in(_rk, 511), 0.3 * jnp.ones((16,), jnp.float32), (32, 361))
        _ctx_2048t = jnp.einsum('bsk,bkd->bsd', _ctx_2048c, _ctx_2048P)
        _ctx_2048t = _ctx_2048t * jax.lax.rsqrt(jnp.mean(jnp.square(_ctx_2048t)) + 1e-12) * 0.953939
        ctx_2048 = -0.000514642 + 1.00011 * (_ctx_2048t + 0.3 * jax.random.normal(jax.random.fold_in(_rk, 611), (32, 361, 512), jnp.float32))
        _validS = jnp.arange(100)[None, :] < _lenS[:, None]
        _validS2 = jnp.arange(361)[None, :] < _lenS2[:, None]
        _causal = jnp.tril(jnp.ones((100, 100), dtype=bool))
        mask_BxS2_bk0 = jnp.logical_not(jnp.broadcast_to(_validS2[:, :], (32, 361)))
        _g = jax.random.normal(jax.random.fold_in(_rk, 9001), (2, 1), jnp.float32)
        _g = jnp.sign(_g) * jnp.maximum(jnp.abs(_g), 1.0) + (_g == 0) * 1.0
        g_xattn = _g[0]
        g_ffn = _g[1]
        return (x, ctx_2048, mask_BxS2_bk0, g_xattn, g_ffn)
    x, ctx_2048, mask_BxS2_bk0, g_xattn, g_ffn = _rec_inputs()

    def _L0_xattn_setup():
        import jax, jax.numpy as jnp
        import numpy as np
        key = jax.random.key(seed)
        k1, k2, k3 = jax.random.split(key, 3)
        B, S, D, M = (8, 512, 512, 128)
        hidden_states = jax.random.normal(k1, (B, S, D), dtype=jnp.float32)
        memory_tokens = jax.random.normal(k2, (B, M, D), dtype=jnp.float32)
        memory_mask = jax.random.randint(k3, (B, M), 0, 2).astype(jnp.bool_)
        return {'hidden_states': hidden_states, 'memory_tokens': memory_tokens, 'memory_mask': memory_mask}
    _L0_xattn_all = _L0_xattn_setup()
    _L0_xattn_in = {k: v for k, v in _L0_xattn_all.items() if k in ()}
    del _L0_xattn_all

    def _L0_ffn_setup():
        import jax, jax.numpy as jnp
        import numpy as np
        D_MODEL = 512
        HIDDEN = int(2 * D_MODEL * 4 / 3)

        def ternary_quant(w):
            s = jnp.mean(jnp.abs(w))
            q = jnp.clip(jnp.round(w / s), -1.0, 1.0) * s
            return w + jax.lax.stop_gradient(q - w)
        key = jax.random.key(seed)
        k0, k1, k2, k3 = jax.random.split(key, 4)
        x = jax.random.normal(k0, (4, 1024, D_MODEL), dtype=jnp.float32)
        std_in = 1.0 / np.sqrt(D_MODEL)
        std_h = 1.0 / np.sqrt(HIDDEN)
        w1 = jax.random.uniform(k1, (HIDDEN, D_MODEL), jnp.float32, -std_in, std_in)
        w3 = jax.random.uniform(k2, (HIDDEN, D_MODEL), jnp.float32, -std_in, std_in)
        w2 = jax.random.uniform(k3, (D_MODEL, HIDDEN), jnp.float32, -std_h, std_h)
        return {'x': x, 'w1': w1, 'w3': w3, 'w2': w2}
    _L0_ffn_all = _L0_ffn_setup()
    _L0_ffn_in = {k: v for k, v in _L0_ffn_all.items() if k in ('w1', 'w3', 'w2')}
    del _L0_ffn_all
    return {'x': x, 'ctx_2048': ctx_2048, 'mask_BxS2_bk0': mask_BxS2_bk0, 'g_xattn': g_xattn, 'g_ffn': g_ffn, 'L0_ffn_w1': _L0_ffn_in['w1'], 'L0_ffn_w3': _L0_ffn_in['w3'], 'L0_ffn_w2': _L0_ffn_in['w2']}

def reference(x, ctx_2048, mask_BxS2_bk0, g_xattn, g_ffn, L0_ffn_w1, L0_ffn_w3, L0_ffn_w2):
    import jax
    import jax.numpy as jnp

    def _L0_xattn_ref(hidden_states, memory_tokens, memory_mask):
        import jax, jax.numpy as jnp
        import numpy as np
        B, S, D = hidden_states.shape
        scale = 1.0 / jnp.sqrt(jnp.asarray(D, hidden_states.dtype))
        scores = jnp.einsum('bsd,bmd->bsm', hidden_states, memory_tokens) * scale
        neg_inf = jnp.asarray(-1e+30, scores.dtype)
        scores = jnp.where(memory_mask[:, None, :], scores, neg_inf)
        attn = jax.nn.softmax(scores, axis=-1)
        readout = jnp.einsum('bsm,bmd->bsd', attn, memory_tokens)
        valid_b = jnp.any(memory_mask, axis=-1)
        out = jnp.where(valid_b[:, None, None], readout, jnp.zeros_like(readout))
        return out

    def _L0_ffn_ref(x, w1, w3, w2):
        import jax, jax.numpy as jnp
        import numpy as np
        D_MODEL = 512
        HIDDEN = int(2 * D_MODEL * 4 / 3)

        def ternary_quant(w):
            s = jnp.mean(jnp.abs(w))
            q = jnp.clip(jnp.round(w / s), -1.0, 1.0) * s
            return w + jax.lax.stop_gradient(q - w)
        w1q = ternary_quant(w1)
        w3q = ternary_quant(w3)
        w2q = ternary_quant(w2)
        h1 = jnp.einsum('bsd,hd->bsh', x, w1q)
        h3 = jnp.einsum('bsd,hd->bsh', x, w3q)
        g = jax.nn.silu(h1) * h3
        return jnp.einsum('bsh,dh->bsd', g, w2q)
    x = x + jnp.tanh(g_xattn[0]) * _L0_xattn_ref(_layernorm(x, axis=-1), ctx_2048, mask_BxS2_bk0)
    x = x + jnp.tanh(g_ffn[0]) * _L0_ffn_ref(_layernorm(x, axis=-1), L0_ffn_w1, L0_ffn_w3, L0_ffn_w2)
    return x

_drawn_inputs = setup_inputs


def setup_inputs(seed=0):
    import zlib

    import numpy as np

    out = dict(_drawn_inputs(seed))
    spreads = {}
    factors = {}
    for name, (base, spread) in spreads.items():
        noise = np.random.default_rng([zlib.crc32(name.encode()), seed]).standard_normal(out[name].shape)
        drawn = base * np.exp(spread * noise) if base else spread * noise
        out[name] = jnp.asarray(drawn.astype(out[name].dtype))
    for name, factor in factors.items():
        out[name] = (out[name] * factor).astype(out[name].dtype)
    return out
```

```python
import concourse.bass as bass
from concourse import mybir
from contextlib import ExitStack


class Group:

    def __init__(self, g, parity, half, first):
        self.g, self.parity, self.half, self.first = g, parity, half, first


def static_group(g):
    return Group(g, g % 2, g // 2, g == 0)


def gated_block(nc, x, ctx_in, mask, g_xattn, g_ffn, w1, w3, w2, out):
    fp32, fp16 = mybir.dt.float32, mybir.dt.float16
    u8 = mybir.dt.uint8
    ALU = mybir.AluOpType
    ACT = mybir.ActivationFunctionType
    AX = mybir.AxisListType

    B, S, D = x.shape
    M = ctx_in.shape[1]
    H = w1.shape[0]
    P = 128
    DC = D // P
    MC = -(-M // P)
    MR = M - (MC - 1) * P
    HC = -(-H // P)
    HR = H - (HC - 1) * P
    HP = HC * P
    GB = 4
    NG = B // GB
    NT = GB * S
    EPS = 1e-5
    XS = 1024.0
    GS = 0.125
    NEG = -1e30
    SCALE = float(D) ** -0.5
    N_W = float(H * D)

    HSLOTS = 2 * HC
    YSLOTS = 2 * DC
    SLOTS = HSLOTS + YSLOTS
    BASE = [2, 8, 15, 21]
    STEPS = [("x1T", 0), ("cT0", 0), ("cT1", 1), ("cT2", 1), ("cT3", 2), ("scores", 3), ("PT", 5),
             ("readout", 6), ("x2T", 8)]
    SMAX, SEXP, X1, LN2 = 3, 4, 6, 7
    T_STEPS = ("x1T", "cT0", "cT1", "cT2", "cT3", "PT", "x2T")
    NTB = 2
    NUB = 4

    def steps_at(s):
        return [(k, name) for k in range(GB) for name, off in STEPS if BASE[k] + off == s]

    T_ORDER = [(k, name) for s in range(SLOTS) for k, name in steps_at(s) if name in T_STEPS]
    assert len(T_ORDER) == GB * len(T_STEPS) and len(T_ORDER) % NTB == 0
    U_ORDER = [(kind, c) for c in range(HC) for kind in ("u1", "u3")]
    U_ORDER += [("yT", c) for c in range(DC)] + [("out", k) for k in range(GB)]
    assert 2 * len(U_ORDER) % NUB == 0

    ctx = ExitStack()
    with ctx:
        def sb(name, shape, dt=fp32):
            return ctx.enter_context(nc.sbuf_tensor(name, shape, dt))

        def sem(name):
            return ctx.enter_context(nc.semaphore(name))

        x_in = [sb(f"x_in{k}", [S, D]) for k in range(GB)]
        c_in = [sb(f"c_in{k}", [P, MC, D]) for k in range(GB)]
        mask_in = [sb(f"mask_in{p}", [S, GB * M], u8) for p in range(2)]
        bias = [sb(f"bias{p}", [S, GB * M]) for p in range(2)]
        xh1 = [sb(f"xh1_{i}", [S, D]) for i in range(2)]
        xT1 = [sb(f"xT1_{i}", [P, DC, S]) for i in range(2)]
        cT = [sb(f"cT_{i}", [P, DC, M]) for i in range(2)]
        score = [sb(f"score_{i}", [S, M]) for i in range(2)]
        prob = [sb(f"prob_{i}", [S, MC * P]) for i in range(2)]
        probT = [sb(f"probT_{i}", [P, MC, S]) for i in range(2)]
        xh2 = [sb(f"xh2_{i}", [S, D]) for i in range(2)]
        x1 = [[sb(f"x1_{p}{k}", [S, D]) for k in range(GB)] for p in range(2)]
        x2hi = [sb(f"x2hi{p}", [P, DC, NT], fp16) for p in range(2)]
        x2lo = [sb(f"x2lo{p}", [P, DC, NT], fp16) for p in range(2)]
        st1 = [sb(f"st1_{i}", [S, 6]) for i in range(2)]
        mv1 = [sb(f"mv1_{i}", [S, 2]) for i in range(2)]
        rs1 = [sb(f"rs1_{i}", [S, 2]) for i in range(2)]
        st2 = [sb(f"st2_{i}", [S, 6]) for i in range(2)]
        mv2 = [sb(f"mv2_{i}", [S, 2]) for i in range(2)]
        rs2 = [sb(f"rs2_{i}", [S, 2]) for i in range(2)]
        smax = [sb(f"smax_{i}", [S, 1]) for i in range(2)]
        nmax = [sb(f"nmax_{i}", [S, 1]) for i in range(2)]
        gate = [sb(f"gate_{i}", [S, 1]) for i in range(2)]
        rsum = [sb(f"rsum_{i}", [S, 1]) for i in range(2)]
        rinv = [sb(f"rinv_{i}", [S, 1]) for i in range(2)]
        alpha = [sb(f"alpha_{i}", [S, 1]) for i in range(2)]
        work = sb("work", [P, max(6 * NT + DC * NT + GB * D, HC * D)])
        wraw = work[:, 0:HC * D]
        th, au, gf = [[work[:, (2 * n + i) * NT:(2 * n + i + 1) * NT] for i in range(2)] for n in range(3)]
        yT = work[:, 6 * NT:(6 + DC) * NT].rearrange("p (c t) -> p c t", t=NT)
        fin = [work[0:S, (6 + DC) * NT + k * D:(6 + DC) * NT + (k + 1) * D] for k in range(GB)]
        quant = sb("quant", [P, 2, HC * D], fp16)
        wneg, wq = quant[:, 0, :], quant[:, 1, :]
        ghi = quant[:, 0, 0:HC * NT].rearrange("p (c t) -> p c t", t=NT)
        glo = quant[:, 1, 0:HC * NT].rearrange("p (c t) -> p c t", t=NT)
        w1T = sb("w1T", [P, DC, HP], fp16)
        w3T = sb("w3T", [P, DC, HP], fp16)
        w2T = sb("w2T", [P, HC, D], fp16)
        asum = sb("asum", [P, 3, HC])
        tot = sb("tot", [P, 3])
        half = sb("half", [P, 3])
        nhalf = sb("nhalf", [P, 3])
        ident = sb("ident", [P, P])
        identh = sb("identh", [P, P], fp16)
        ones = sb("ones", [P, P])
        power = sb("power", [P, 1])
        gates = sb("gates", [P, 2])
        tgates = sb("tgates", [P, 2])
        c_tanh = sb("c_tanh", [P, 1])
        beta = sb("beta", [P, 1])
        btmp = sb("btmp", [P, 2])

        def bank(name):
            return ctx.enter_context(nc.psum_tensor(name, [P, 512], fp32))

        Tb = [bank(f"Tb{i}") for i in range(NTB)]
        Sb = bank("Sb")
        Rb = bank("Rb")
        Ub = [bank(f"Ub{i}") for i in range(NUB)]

        x_loaded = [sem(f"x_loaded{k}") for k in range(GB)]
        c_loaded = [sem(f"c_loaded{k}") for k in range(GB)]
        mask_loaded = [sem(f"mask_loaded{p}") for p in range(2)]
        w_loaded = sem("w_loaded")
        gates_loaded = sem("gates_loaded")
        stored = [sem(f"stored{k}") for k in range(GB)]
        consts_ready = sem("consts_ready")
        wpad_ready = sem("wpad_ready")
        setup_done = sem("setup_done")
        setup_chain = sem("setup_chain")
        tanh_ready = sem("tanh_ready")
        asum_ready = sem("asum_ready")
        tot_ready = sem("tot_ready")
        wq_ready = sem("wq_ready")
        wt_ready = sem("wt_ready")
        wt_done = sem("wt_done")
        coef_ready = sem("coef_ready")
        bias_ready = sem("bias_ready")
        stats1 = sem("stats1")
        rstd1 = sem("rstd1")
        xh1_ready = sem("xh1_ready")
        t_ready = sem("t_ready")
        xT1_ready = sem("xT1_ready")
        cT_ready = sem("cT_ready")
        scores_ready = sem("scores_ready")
        masked_ready = sem("masked_ready")
        nmax_ready = sem("nmax_ready")
        gate_ready = sem("gate_ready")
        prob_ready = sem("prob_ready")
        rinv_ready = sem("rinv_ready")
        alpha_ready = sem("alpha_ready")
        probT_ready = sem("probT_ready")
        readout_ready = sem("readout_ready")
        x1_ready = sem("x1_ready")
        stats2 = sem("stats2")
        rstd2 = sem("rstd2")
        xh2_ready = sem("xh2_ready")
        x2hi_ready = sem("x2hi_ready")
        x2lo_ready = sem("x2lo_ready")
        ln_chain = sem("ln_chain")
        pool_chain = sem("pool_chain")
        u1_ready = sem("u1_ready")
        u3_ready = sem("u3_ready")
        th_ready = sem("th_ready")
        au_ready = sem("au_ready")
        gf_ready = sem("gf_ready")
        ghi_ready = sem("ghi_ready")
        glo_ready = sem("glo_ready")
        yps_ready = sem("yps_ready")
        yT_ready = sem("yT_ready")
        out_ready = sem("out_ready")
        fin_ready = sem("fin_ready")

        block = ctx.enter_context(nc.Block())

        def nb(G, k):
            return G.g * GB + (k + 1)

        def nh(G, c):
            return G.g * HC + (c + 1)

        def nt(G, pos):
            return G.g * len(T_ORDER) + (pos + 1)

        def t_released(G, k, name):
            if name == "x1T":
                return xT1_ready, nb(G, k)
            if name.startswith("cT"):
                return cT_ready, (G.g * GB + k) * DC + int(name[2]) + 1
            if name == "PT":
                return probT_ready, nb(G, k)
            return x2lo_ready, nb(G, k)

        def wait_alone(eng, semaphore, value):
            if not isinstance(value, int):
                value = eng.to_reg(value)
            eng.wait_ge(setup_done, 1)
            eng.wait_ge(semaphore, value)

        def before(G):
            return Group(G.g - 1, 1 - G.parity, None, False)

        def wait_t_bank(eng, G, pos):
            if pos >= NTB:
                eng.wait_ge(*t_released(G, *T_ORDER[pos - NTB]))
            elif not G.first:
                eng.wait_ge(*t_released(before(G), *T_ORDER[pos - NTB]))

        def u_released(G, kind, c):
            if kind == "u1":
                return au_ready, nh(G, c)
            if kind == "u3":
                return gf_ready, nh(G, c)
            if kind == "yT":
                return yT_ready, G.g * DC + (c + 1)
            return fin_ready, nb(G, c)

        def wait_u_bank(eng, G, pos):
            if pos >= NUB:
                eng.wait_ge(*u_released(G, *U_ORDER[pos - NUB]))
            elif not G.first:
                eng.wait_ge(*u_released(before(G), *U_ORDER[pos - NUB]))

        def t_bank(k, name):
            return Tb[T_ORDER.index((k, name)) % NTB]

        def u_bank(G, kind, c):
            return Ub[(U_ORDER.index((kind, c)) + len(U_ORDER) * G.parity) % NUB]

        def w_rows(w):
            return w[0:(HC - 1) * P, :].rearrange("(c p) d -> p c d", p=P)

        @block.sync
        def _(sp):
            def load_batch(G, k):
                b = G.g * GB + k
                sp.dma_start(x_in[k][:, :], x[bass.ds(b, 1), :, :].rearrange("a s d -> (a s) d")).then_inc(x_loaded[k], 16)
                src = ctx_in[bass.ds(b, 1), :, :].rearrange("a m d -> (a m) d")
                sp.dma_start(c_in[k][:, 0:MC - 1, :],
                             src[0:(MC - 1) * P, :].rearrange("(c p) d -> p c d", p=P)).then_inc(c_loaded[k], 16)
                sp.dma_start(c_in[k][0:MR, MC - 1, :], src[(MC - 1) * P:M, :]).then_inc(c_loaded[k], 16)

            def load_mask(G):
                b = G.g * GB
                rows = mask[bass.ds(b, GB), :].rearrange("(a b) m -> a (b m)", a=1)
                sp.dma_start(mask_in[G.parity][:, :], rows.broadcast_to([S, GB * M])).then_inc(mask_loaded[G.parity], 16)

            def store_batch(G, k):
                b = G.g * GB + k
                sp.wait_ge(fin_ready, nb(G, k))
                sp.dma_start(out[bass.ds(b, 1), :, :].rearrange("a s d -> (a s) d"), fin[k]).then_inc(stored[k], 16)

            first = static_group(0)
            for k in range(GB):
                load_batch(first, k)
                if k == 0:
                    load_mask(first)
            sp.dma_start(gates[:, 0:1], g_xattn.rearrange("(a b) -> a b", a=1).broadcast_to([P, 1])).then_inc(gates_loaded, 16)
            sp.dma_start(gates[:, 1:2], g_ffn.rearrange("(a b) -> a b", a=1).broadcast_to([P, 1])).then_inc(gates_loaded, 16)
            for n, w in enumerate((w1, w3, w2)):
                if n == 0:
                    sp.wait_ge(wpad_ready, 1)
                else:
                    sp.wait_ge(wq_ready, n)
                    if n == 2:
                        sp.wait_ge(wpad_ready, 2)
                if n < 2:
                    dst = wraw.rearrange("p (c d) -> p c d", d=D)
                    sp.dma_start(dst[:, 0:HC - 1, :], w_rows(w)).then_inc(w_loaded, 16)
                    sp.dma_start(dst[0:HR, HC - 1, :], w[(HC - 1) * P:H, :]).then_inc(w_loaded, 16)
                else:
                    dst = wraw.rearrange("p (c h) -> p c h", h=HP)
                    sp.dma_start(dst[:, 0:2, 0:H], w[0:2 * P, :].rearrange("(c p) h -> p c h", p=P)).then_inc(w_loaded, 16)
                    sp.dma_start(dst[:, 2:4, 0:H], w[2 * P:4 * P, :].rearrange("(c p) h -> p c h", p=P)).then_inc(w_loaded, 16)

            def stretch(F, A):
                if A is not None:
                    nxt = Group(A.g + 1, 1 - A.parity, None, False)
                    if isinstance(A.g, int) and A.g == NG - 1:
                        nxt = None
                    if nxt is not None:
                        if A.first is False:
                            sp.wait_ge(bias_ready, A.g)
                        load_mask(nxt)
                        for k in range(GB):
                            sp.wait_ge(x1_ready, nb(A, k))
                            load_batch(nxt, k)
                if F is not None:
                    for k in range(GB):
                        store_batch(F, k)

            stretch(None, static_group(0))
            stretch(static_group(0), static_group(1))
            n_loop = (NG - 2) // 2
            with nc.Fori(0, n_loop - 1, engines=[sp.engine], hint_back_edge=True) as j:
                stretch(Group(j * 2 + 1, 1, j, False), Group(j * 2 + 2, 0, j + 1, False))
                stretch(Group(j * 2 + 2, 0, j + 1, False), Group(j * 2 + 3, 1, j + 1, False))
            stretch(static_group(NG - 3), static_group(NG - 2))
            stretch(static_group(NG - 2), static_group(NG - 1))
            stretch(static_group(NG - 1), None)
            for k in range(GB):
                sp.wait_ge(stored[k], 16 * NG)

        @block.gpsimd
        def _(pool):
            pool.memset(ident[:, :], 0.0).then_inc(setup_done, 1)
            pool.wait_ge(setup_done, 1)
            pool.affine_select(out=ident[:, :], in_=ident[:, :], compare_op=ALU.not_equal, fill=1.0, base=0,
                               pattern=[[-1, P]], channel_multiplier=1).then_inc(pool_chain, 1)
            pool.wait_ge(pool_chain, 1)
            pool.tensor_copy(identh[:, :], ident[:, :]).then_inc(consts_ready, 1)
            pool.memset(ones[:, :], 1.0).then_inc(consts_ready, 1)
            pool.memset(power[:, :], -0.5).then_inc(consts_ready, 1)
            for i in range(2):
                pool.memset(prob[i][:, M:MC * P], 0.0).then_inc(consts_ready, 1)
            pool.wait_ge(consts_ready, 5)
            pool.memset(wraw[:, (HC - 1) * D:HC * D], 0.0).then_inc(wpad_ready, 1)

            def bias_of(G):
                wait_alone(pool, mask_loaded[G.parity], (G.half + 1) * 16)
                pool.tensor_scalar(bias[G.parity][:, :], mask_in[G.parity][:, :], -NEG, NEG, ALU.mult, ALU.add)\
                    .then_inc(bias_ready, 1)

            def rstd(G, k, which):
                i = k % 2
                mv, rs = (mv1, rs1) if which == 1 else (mv2, rs2)
                pool.wait_ge(stats1 if which == 1 else stats2, nb(G, k))
                pool.tensor_tensor(rs[i][:, 0:1], mv[i][:, 1:2], power[0:S, :], ALU.pow)\
                    .then_inc(rstd1 if which == 1 else rstd2, 1)

            def stretch(F, A):
                if A is None:
                    return
                bias_of(A)
                for s in range(SLOTS):
                    for k in range(GB):
                        if s == BASE[k] - 2:
                            rstd(A, k, 1)
                        if s == BASE[k] + X1:
                            rstd(A, k, 2)

            stretch(None, static_group(0))
            pool.wait_ge(wq_ready, 2)
            pool.memset(wraw.rearrange("p (c h) -> p c h", h=HP)[:, :, H:HP], 0.0).then_inc(wpad_ready, 1)
            stretch(static_group(0), static_group(1))
            with nc.Fori(0, (NG - 2) // 2, engines=[pool.engine], hint_back_edge=True) as j:
                stretch(None, Group(j * 2 + 2, 0, j + 1, False))
                stretch(None, Group(j * 2 + 3, 1, j + 1, False))

        @block.scalar
        def _(act):
            act.wait_ge(gates_loaded, 32)
            act.activation(tgates[:, :], gates[:, :], ACT.Tanh).then_inc(tanh_ready, 1)

            def read_t(G, k, name):
                i = k % 2
                src = t_bank(k, name)
                act.wait_ge(t_ready, nt(G, T_ORDER.index((k, name))))
                if name == "x1T":
                    act.activation(xT1[i][:, :, :], src[:, 0:DC * S].rearrange("p (c s) -> p c s", s=S), ACT.Copy)\
                        .then_inc(xT1_ready, 1)
                elif name.startswith("cT"):
                    act.activation(cT[i][:, int(name[2]), :], src[:, 0:M], ACT.Copy).then_inc(cT_ready, 1)
                elif name == "PT":
                    act.activation(probT[i][:, :, :], src[:, 0:MC * S].rearrange("p (c s) -> p c s", s=S), ACT.Copy)\
                        .then_inc(probT_ready, 1)
                else:
                    act.activation(x2hi[G.parity][:, :, k * S:(k + 1) * S],
                                   src[:, 0:DC * S].rearrange("p (c s) -> p c s", s=S), ACT.Copy, scale=XS)\
                        .then_inc(x2hi_ready, 1)

            def softmax_exp(G, k):
                i = k % 2
                act.wait_ge(nmax_ready, nb(G, k))
                act.activation(prob[i][:, 0:M], score[i][:, :], ACT.Exp, bias=nmax[i][:, :], scale=SCALE,
                               accum_out=rsum[i][:, :]).then_inc(prob_ready, 1)

            def gate_tanh(G, c):
                act.wait_ge(u1_ready, nh(G, c))
                act.activation(th[c % 2], u_bank(G, "u1", c)[:, 0:NT], ACT.Tanh, scale=c_tanh[:, :])\
                    .then_inc(th_ready, 1)

            def high_part(G, c):
                act.wait_ge(gf_ready, nh(G, c))
                act.activation(ghi[:, c, :], gf[c % 2], ACT.Copy).then_inc(ghi_ready, 1)

            def read_y(G, c):
                act.wait_ge(yps_ready, G.g * DC + (c + 1))
                act.activation(yT[:, c, :], u_bank(G, "yT", c)[:, 0:NT], ACT.Copy).then_inc(yT_ready, 1)

            def stretch(F, A):
                for s in range(SLOTS):
                    if F is not None and s < HSLOTS and s % 2 == 1:
                        gate_tanh(F, s // 2)
                    if A is not None:
                        for k, name in steps_at(s):
                            if name in T_STEPS:
                                read_t(A, k, name)
                        for k in range(GB):
                            if s == BASE[k] + SEXP:
                                softmax_exp(A, k)
                    if F is not None:
                        if 2 <= s <= HSLOTS and s % 2 == 0:
                            high_part(F, s // 2 - 1)
                        if s > HSLOTS and (s - HSLOTS) % 2 == 0:
                            read_y(F, (s - HSLOTS) // 2 - 1)
                if F is not None:
                    read_y(F, DC - 1)

            stretch(None, static_group(0))
            for n in range(3 * HC):
                act.wait_ge(wt_ready, n + 1)
                m, c = n // HC, n % HC
                src = Ub[n % NUB][:, 0:DC * P // 2].bitcast(fp16)
                if m < 2:
                    dst = (w1T, w3T)[m][:, :, c * P:(c + 1) * P]
                    src = src.rearrange("p (c h) -> p c h", h=P)
                else:
                    dst = w2T[:, c, :]
                act.activation(dst, src, ACT.Copy).then_inc(wt_done, 1)
            act.wait_ge(coef_ready, 1)
            stretch(static_group(0), static_group(1))
            with nc.Fori(0, (NG - 2) // 2, engines=[act.engine], hint_back_edge=True) as j:
                a = Group(j * 2 + 1, 1, j, False)
                b = Group(j * 2 + 2, 0, j + 1, False)
                c = Group(j * 2 + 3, 1, j + 1, False)
                stretch(a, b)
                stretch(b, c)
            stretch(static_group(NG - 1), None)

        @block.vector
        def _(dve):
            chained = [0]

            def link(ins):
                chained[0] += 1
                ins.then_inc(setup_chain, 1)
                dve.wait_ge(setup_chain, chained[0])

            LN_ORDER = sorted([(BASE[k] - 2, k, 1) for k in range(GB)] + [(BASE[k] + X1, k, 2) for k in range(GB)])

            def stats(G, k, which):
                i = k % 2
                at = G.g * (4 * GB) + 2 * [(q, w) for _, q, w in LN_ORDER].index((k, which))
                src, st, mv = (x_in[k], st1[i], mv1[i]) if which == 1 else (x1[G.parity][k], st2[i], mv2[i])
                if which == 1:
                    dve.wait_ge(x_loaded[k], (G.g + 1) * 16)
                else:
                    dve.wait_ge(x1_ready, nb(G, k))
                dve.bn_stats(st[:, :], src[:, :]).then_inc(ln_chain, 1)
                wait_alone(dve, ln_chain, at + 1)
                dve.bn_aggr(mv[:, :], st[:, :]).then_inc(ln_chain, 1)
                dve.wait_ge(ln_chain, at + 2)
                dve.tensor_scalar(mv[:, 1:2], mv[:, 1:2], EPS, None, ALU.add)\
                    .then_inc(stats1 if which == 1 else stats2, 1)

            def normalise(G, k, which):
                i = k % 2
                if which == 1:
                    src, mv, rs, dst, ready, done = x_in[k], mv1[i], rs1[i], xh1[i], rstd1, xh1_ready
                else:
                    src, mv, rs, dst, ready, done = x1[G.parity][k], mv2[i], rs2[i], xh2[i], rstd2, xh2_ready
                dve.wait_ge(ready, nb(G, k))
                dve.tensor_scalar(dst[:, :], src[:, :], mv[:, 0:1], rs[:, 0:1], ALU.subtract, ALU.mult)\
                    .then_inc(done, 1)

            def masked_max(G, k):
                i = k % 2
                wait_alone(dve, scores_ready, nb(G, k))
                if k == 0:
                    dve.wait_ge(bias_ready, G.g + 1)
                dve.tensor_tensor_reduce(out=score[i][:, :], in0=Sb[0:S, 0:M],
                                         in1=bias[G.parity][:, k * M:(k + 1) * M], scale=1.0, scalar=-3e38,
                                         op0=ALU.add, op1=ALU.max, accum_out=smax[i][:, :]).then_inc(masked_ready, 1)
                dve.wait_ge(masked_ready, nb(G, k))
                dve.tensor_scalar(nmax[i][:, :], smax[i][:, :], -SCALE, None, ALU.mult).then_inc(nmax_ready, 1)
                dve.tensor_scalar(gate[i][:, :], smax[i][:, :], 0.5 * NEG, tgates[0:S, 0:1], ALU.is_gt, ALU.mult)\
                    .then_inc(gate_ready, 1)

            def first_residual(G, k):
                i = k % 2
                dve.wait_ge(prob_ready, nb(G, k))
                dve.reciprocal(rinv[i][:, :], rsum[i][:, :]).then_inc(rinv_ready, 1)
                dve.wait_ge(rinv_ready, nb(G, k))
                dve.wait_ge(gate_ready, nb(G, k))
                dve.tensor_tensor(alpha[i][:, :], rinv[i][:, :], gate[i][:, :], ALU.mult).then_inc(alpha_ready, 1)
                dve.wait_ge(alpha_ready, nb(G, k))
                dve.wait_ge(readout_ready, nb(G, k))
                dve.scalar_tensor_tensor(x1[G.parity][k][:, :], Rb[0:S, :], alpha[i][:, :], x_in[k][:, :],
                                         ALU.mult, ALU.add).then_inc(x1_ready, 1)

            def x2_low(G, k):
                dve.wait_ge(x2hi_ready, nb(G, k))
                dve.scalar_tensor_tensor(x2lo[G.parity][:, :, k * S:(k + 1) * S],
                                         t_bank(k, "x2T")[:, 0:DC * S].rearrange("p (c s) -> p c s", s=S), XS,
                                         x2hi[G.parity][:, :, k * S:(k + 1) * S], ALU.mult, ALU.subtract)\
                    .then_inc(x2lo_ready, 1)

            def silu_part(G, c):
                dve.wait_ge(th_ready, nh(G, c))
                dve.scalar_tensor_tensor(au[c % 2], th[c % 2], 1.0, u_bank(G, "u1", c)[:, 0:NT],
                                         ALU.add, ALU.mult).then_inc(au_ready, 1)

            def gated(G, c):
                dve.wait_ge(au_ready, nh(G, c))
                dve.wait_ge(u3_ready, nh(G, c))
                dve.scalar_tensor_tensor(gf[c % 2], au[c % 2], GS / (2 * XS * XS),
                                         u_bank(G, "u3", c)[:, 0:NT], ALU.mult, ALU.mult).then_inc(gf_ready, 1)

            def low_part(G, c):
                dve.wait_ge(ghi_ready, nh(G, c))
                dve.tensor_tensor(glo[:, c, :], gf[c % 2], ghi[:, c, :], ALU.subtract).then_inc(glo_ready, 1)

            def second_residual(G, k):
                dve.wait_ge(out_ready, nb(G, k))
                if not G.first:
                    dve.wait_ge(stored[k], G.g * 16)
                dve.scalar_tensor_tensor(fin[k], u_bank(G, "out", k)[0:S, :], beta[0:S, :],
                                         x1[G.parity][k][:, :], ALU.mult, ALU.add).then_inc(fin_ready, 1)

            def stretch(F, A):
                for s in range(SLOTS):
                    if F is not None and s < HSLOTS and s % 2 == 1:
                        silu_part(F, s // 2)
                    if F is not None and 2 <= s <= HSLOTS and s % 2 == 0:
                        gated(F, s // 2 - 1)
                    if F is not None and 3 <= s <= HSLOTS + 1 and s % 2 == 1:
                        low_part(F, s // 2 - 1)
                    if A is not None:
                        for k in range(GB):
                            if s == BASE[k] - 2:
                                stats(A, k, 1)
                            if s == BASE[k] - 1:
                                normalise(A, k, 1)
                            if s == BASE[k] + SMAX:
                                masked_max(A, k)
                            if s == BASE[k] + X1:
                                first_residual(A, k)
                                stats(A, k, 2)
                            if s == BASE[k] + LN2:
                                normalise(A, k, 2)
                            if s == BASE[k] + LN2 + 1:
                                x2_low(A, k)
                if F is not None:
                    for k in range(GB):
                        second_residual(F, k)

            dve.wait_ge(tanh_ready, 1)
            stretch(None, static_group(0))
            for n in range(3):
                dve.wait_ge(w_loaded, 32 * (n + 1))
                if n == 2:
                    dve.wait_ge(wpad_ready, 2)
                dve.tensor_reduce(asum[:, n, :], wraw.rearrange("p (c d) -> p c d", c=HC), AX.X, ALU.add,
                                  apply_absolute_value=True).then_inc(asum_ready, 1)
                dve.wait_ge(tot_ready, n + 1)
                link(dve.tensor_reduce(tot[:, n:n + 1], Rb[:, n * HC:(n + 1) * HC], AX.X, ALU.add))
                link(dve.tensor_scalar(half[:, n:n + 1], tot[:, n:n + 1], 1.0 / N_W, 0.5, ALU.mult, ALU.mult))
                link(dve.tensor_scalar(nhalf[:, n:n + 1], half[:, n:n + 1], -1.0, None, ALU.mult))
                link(dve.tensor_scalar(wneg, wraw, nhalf[:, n:n + 1], None, ALU.is_lt))
                if n >= 1:
                    dve.wait_ge(wt_ready, HC * n)
                dve.scalar_tensor_tensor(wq, wraw, half[:, n:n + 1], wneg, ALU.is_gt, ALU.subtract)\
                    .then_inc(wq_ready, 1)
            dve.tensor_scalar(c_tanh[:, :], half[:, 0:1], 1.0 / XS, None, ALU.mult).then_inc(coef_ready, 1)
            link(dve.tensor_tensor(btmp[:, 0:1], half[:, 0:1], half[:, 1:2], ALU.mult))
            link(dve.tensor_tensor(btmp[:, 1:2], btmp[:, 0:1], half[:, 2:3], ALU.mult))
            link(dve.tensor_scalar(beta[:, :], btmp[:, 1:2], tgates[:, 1:2], 8.0 / GS, ALU.mult, ALU.mult))
            stretch(static_group(0), static_group(1))
            with nc.Fori(0, (NG - 2) // 2, engines=[dve.engine], hint_back_edge=True) as j:
                a = Group(j * 2 + 1, 1, j, False)
                b = Group(j * 2 + 2, 0, j + 1, False)
                c = Group(j * 2 + 3, 1, j + 1, False)
                stretch(a, b)
                stretch(b, c)
            stretch(static_group(NG - 1), None)

        @block.tensor
        def _(pe):
            mrows = [P] * (MC - 1) + [MR]

            def attention_step(G, k, name):
                i = k % 2
                if name in T_STEPS:
                    pos = T_ORDER.index((k, name))
                    dst = t_bank(k, name)
                    wait_t_bank(pe, G, pos)
                if name == "x1T":
                    pe.wait_ge(xh1_ready, nb(G, k))
                    for c in range(DC):
                        last = pe.transpose(dst[:, c * S:(c + 1) * S], xh1[i][:, c * P:(c + 1) * P], ident[0:S, 0:S])
                    last.then_inc(t_ready, 1)
                elif name.startswith("cT"):
                    d = int(name[2])
                    if d == 0:
                        pe.wait_ge(c_loaded[k], (G.g + 1) * 32)
                    for m, rows in enumerate(mrows):
                        last = pe.transpose(dst[:, m * P:m * P + rows], c_in[k][0:rows, m, d * P:(d + 1) * P],
                                            ident[0:rows, 0:rows])
                    last.then_inc(t_ready, 1)
                elif name == "scores":
                    pe.wait_ge(xT1_ready, nb(G, k))
                    pe.wait_ge(cT_ready, nb(G, k) * DC)
                    if k or not G.first:
                        pe.wait_ge(masked_ready, G.g * GB + k)
                    for c in range(DC):
                        last = pe.matmul(Sb[0:S, 0:M], xT1[i][:, c, :], cT[i][:, c, :], start=c == 0, stop=c == DC - 1)
                    last.then_inc(scores_ready, 1)
                elif name == "PT":
                    pe.wait_ge(prob_ready, nb(G, k))
                    for m in range(MC):
                        last = pe.transpose(dst[:, m * S:(m + 1) * S], prob[i][:, m * P:(m + 1) * P], ident[0:S, 0:S])
                    last.then_inc(t_ready, 1)
                elif name == "readout":
                    pe.wait_ge(probT_ready, nb(G, k))
                    if k or not G.first:
                        pe.wait_ge(x1_ready, G.g * GB + k)
                    for m, rows in enumerate(mrows):
                        last = pe.matmul(Rb[0:S, :], probT[i][0:rows, m, :], c_in[k][0:rows, m, :],
                                         start=m == 0, stop=m == MC - 1)
                    last.then_inc(readout_ready, 1)
                else:
                    pe.wait_ge(xh2_ready, nb(G, k))
                    for c in range(DC):
                        last = pe.transpose(dst[:, c * S:(c + 1) * S], xh2[i][:, c * P:(c + 1) * P], ident[0:S, 0:S])
                    last.then_inc(t_ready, 1)

            def project(G, s):
                c, kind = s // 2, ("u1", "u3")[s % 2]
                w, ready = (w1T, u1_ready) if kind == "u1" else (w3T, u3_ready)
                dst = u_bank(G, kind, c)
                wait_u_bank(pe, G, U_ORDER.index((kind, c)))
                if s == 0:
                    pe.wait_ge(x2lo_ready, nb(G, GB - 1))
                for d in range(DC):
                    for part in (x2hi, x2lo):
                        last = pe.matmul(dst[:, 0:NT], w[:, d, c * P:(c + 1) * P], part[G.parity][:, d, :],
                                         start=d == 0 and part is x2hi, stop=d == DC - 1 and part is x2lo)
                last.then_inc(ready, 1)

            def down(G, s):
                d, part = (s - HSLOTS) // 2, (s - HSLOTS) % 2
                dst = u_bank(G, "yT", d)
                mid = (HC + 1) // 2
                if part == 0:
                    wait_u_bank(pe, G, U_ORDER.index(("yT", d)))
                for c in range(0, mid) if part == 0 else range(mid, HC):
                    if d == 0:
                        pe.wait_ge(glo_ready, nh(G, c))
                    for g in (ghi, glo):
                        last = pe.matmul(dst[:, 0:NT], w2T[:, c, d * P:(d + 1) * P], g[:, c, :],
                                         start=c == 0 and g is ghi, stop=c == HC - 1 and g is glo)
                if part == 1:
                    last.then_inc(yps_ready, 1)

            def output(G, k):
                wait_u_bank(pe, G, U_ORDER.index(("out", k)))
                if k == 0:
                    pe.wait_ge(yT_ready, (G.g + 1) * DC)
                dst = u_bank(G, "out", k)
                for d in range(DC):
                    last = pe.transpose(dst[0:S, d * P:(d + 1) * P], yT[:, d, k * S:(k + 1) * S], ident[:, :])
                last.then_inc(out_ready, 1)

            def stretch(F, A):
                for s in range(SLOTS):
                    if A is not None:
                        for k, name in steps_at(s):
                            attention_step(A, k, name)
                    if F is not None:
                        if s < HSLOTS:
                            project(F, s)
                        else:
                            down(F, s)
                if F is not None:
                    for k in range(GB):
                        output(F, k)

            pe.wait_ge(consts_ready, 5)
            stretch(None, static_group(0))
            for n in range(3):
                pe.wait_ge(asum_ready, n + 1)
                if n == 0:
                    pe.wait_ge(x1_ready, GB)
                pe.matmul(Rb[:, n * HC:(n + 1) * HC], ones[:, :], asum[:, n, :], start=True, stop=True)\
                    .then_inc(tot_ready, 1)
                pe.wait_ge(wq_ready, n + 1)
                for c in range(HC):
                    t = n * HC + c
                    if t >= NUB:
                        pe.wait_ge(wt_done, t - NUB + 1)
                    dst = Ub[t % NUB][:, 0:DC * P // 2].bitcast(fp16)
                    for d in range(DC):
                        col = c * D + d * P if n < 2 else d * HP + c * P
                        last = pe.transpose(dst[:, d * P:(d + 1) * P], wq[:, col:col + P], identh[:, :])
                    last.then_inc(wt_ready, 1)
            pe.wait_ge(wt_done, 3 * HC)
            stretch(static_group(0), static_group(1))
            with nc.Fori(0, (NG - 2) // 2, engines=[pe.engine], hint_back_edge=True) as j:
                a = Group(j * 2 + 1, 1, j, False)
                b = Group(j * 2 + 2, 0, j + 1, False)
                c = Group(j * 2 + 3, 1, j + 1, False)
                stretch(a, b)
                stretch(b, c)
            stretch(static_group(NG - 1), None)


_INS = ["x", "ctx_2048", "mask_BxS2_bk0", "g_xattn", "g_ffn", "L0_ffn_w1", "L0_ffn_w3", "L0_ffn_w2"]


def kernel(**inputs):
    import numpy as _np
    import concourse.bacc as _bacc
    from concourse import mybir as _mybir
    from concourse.bass_utils import run_bass_kernel_spmd as _run

    nc = _bacc.Bacc("TRN2", target_bir_lowering=False, num_devices=1)
    arrays, args = {}, []
    for name in _INS:
        a = _np.ascontiguousarray(inputs[name])
        arrays[f"in_{name}_dram"] = a
        args.append(nc.dram_tensor(f"in_{name}_dram", a.shape, _mybir.dt.from_np(a.dtype), kind="ExternalInput").ap())
    shape = inputs["x"].shape
    args.append(nc.dram_tensor("out_0_dram", shape, _mybir.dt.float32, kind="ExternalOutput").ap())
    gated_block(nc, *args)
    r = _run(nc, [arrays], core_ids=[0])
    return r.results[0]["out_0_dram"]
```

```python
import concourse.bass as bass
from concourse import mybir
from contextlib import ExitStack


class Plan:

    def __init__(self, steps, t_steps):
        self.slot = {(k, name): slots[k] for k in range(len(steps["scores"])) for name, slots in steps.items()}
        self.slots = max(self.slot.values()) + 1
        self.t_order = [step for s in range(self.slots) for step in self.at(s, t_steps)]

    def at(self, s, names):
        return [step for step, slot in self.slot.items() if slot == s and step[1] in names]


class Group:

    def __init__(self, g, parity, half, plan, first=False):
        self.g, self.parity, self.half, self.plan, self.first = g, parity, half, plan, first


def gated_block(nc, x, ctx_in, mask, g_xattn, g_ffn, w1, w3, w2, out):
    fp32, fp32r, fp16 = mybir.dt.float32, mybir.dt.float32r, mybir.dt.float16
    u8 = mybir.dt.uint8
    ALU = mybir.AluOpType
    ACT = mybir.ActivationFunctionType
    AX = mybir.AxisListType

    B, S, D = x.shape
    M = ctx_in.shape[1]
    H = w1.shape[0]
    P = 128
    DC = D // P
    MC = -(-M // P)
    MR = M - (MC - 1) * P
    HC = -(-H // P)
    HR = H - (HC - 1) * P
    HP = HC * P
    GB = 4
    NG = B // GB
    NT = GB * S
    EPS = 1e-5
    XS = 1024.0
    GS = 0.125
    NEG = -1e30
    SCALE = float(D) ** -0.5
    N_W = float(H * D)
    MAGIC = 1.5 * 2 ** 23
    MP = M + M % 2

    N_CONSTS = 9
    HSLOTS = 2 * HC
    YSLOTS = 2 * DC
    SLOTS = HSLOTS + YSLOTS
    T_STEPS = ("x1T", "cT0", "cT1", "cT2", "cT3", "PT", "x2T")
    PE_STEPS = T_STEPS + ("scores", "readout")
    OTHER_STEPS = ("stats1", "norm1", "split", "max", "exp", "res1", "norm2")
    STEPS0 = {
        "stats1": [0, 6, 11, 16],
        "norm1": [1, 7, 12, 17],
        "x1T": [2, 8, 13, 18],
        "cT0": [3, 8, 14, 19],
        "cT1": [4, 10, 15, 21],
        "cT2": [5, 11, 16, 21],
        "cT3": [6, 12, 17, 22],
        "scores": [7, 13, 18, 23],
        "split": [7, 12, 18, 23],
        "max": [7, 13, 18, 23],
        "exp": [8, 14, 19, 24],
        "PT": [9, 15, 20, 25],
        "readout": [11, 17, 22, 27],
        "res1": [11, 17, 22, 27],
        "norm2": [12, 18, 23, 28],
        "x2T": [13, 19, 24, 29],
    }
    STEPS1 = {
        "stats1": [0, 5, 12, 17],
        "norm1": [1, 5, 14, 18],
        "x1T": [2, 7, 15, 19],
        "cT0": [1, 6, 14, 20],
        "cT1": [3, 8, 16, 20],
        "cT2": [3, 8, 16, 20],
        "cT3": [4, 9, 17, 21],
        "scores": [6, 11, 19, 23],
        "split": [6, 11, 19, 23],
        "max": [6, 11, 19, 23],
        "exp": [7, 12, 20, 24],
        "PT": [8, 13, 21, 25],
        "readout": [10, 15, 23, 27],
        "res1": [10, 15, 23, 27],
        "norm2": [11, 16, 23, 28],
        "x2T": [12, 17, 25, 29],
    }
    STEPS2 = {
        "stats1": [0, 2, 12, 14],
        "norm1": [2, 6, 14, 18],
        "x1T": [4, 7, 15, 19],
        "cT0": [2, 7, 15, 19],
        "cT1": [4, 8, 16, 20],
        "cT2": [5, 9, 17, 21],
        "cT3": [5, 9, 18, 21],
        "scores": [7, 11, 19, 23],
        "split": [7, 11, 18, 23],
        "max": [7, 11, 19, 24],
        "exp": [8, 12, 20, 24],
        "PT": [10, 14, 22, 26],
        "readout": [11, 15, 23, 27],
        "res1": [11, 15, 23, 27],
        "norm2": [12, 16, 23, 28],
        "x2T": [13, 19, 25, 29],
    }
    PLANS = [Plan(steps, T_STEPS) for steps in (STEPS0, STEPS1, STEPS2)]
    NTB = 2
    NUB = 4
    NTT = GB * len(T_STEPS)
    assert NTT % NTB == 0
    for plan in PLANS:
        assert len(plan.t_order) == NTT and plan.t_order[-NTB:] == PLANS[0].t_order[-NTB:]
    assert all(plan.slots <= SLOTS for plan in PLANS[1:])

    def static_group(g):
        return Group(g, g % 2, g // 2, PLANS[min(g, 2)], g == 0)

    def pair_of_stretches(stretch, j):
        a = Group(j * 2 + 1, 1, j, PLANS[2])
        b = Group(j * 2 + 2, 0, j + 1, PLANS[2])
        c = Group(j * 2 + 3, 1, j + 1, PLANS[2])
        stretch(a, b)
        stretch(b, c)

    U_ORDER = [(kind, c) for c in range(HC) for kind in ("u1", "u3")]
    U_ORDER += [("yT", c) for c in range(DC)] + [("out", k) for k in range(GB)]
    assert 2 * len(U_ORDER) % NUB == 0
    HQ = 4
    W2_TILES = [(d, q) for d in range(DC) for q in range(-(-HC // HQ))]
    W2_SUM = [0, 1, 3, 4]
    W2_TOTALS = [8]
    W2_QUANT = [9, 9, 15, 18]
    W2_PUTS = [13, 16, 21]
    W2_PUT = [(s, n * NUB, (n + 1) * NUB) for n, s in enumerate(W2_PUTS)]
    assert W2_PUT[-1][2] == len(W2_TILES) and W2_PUT[-1][0] < HSLOTS
    CUTS = [0, 3, 6, 9, HC]
    W13_PIECES = [(n, a, b) for n in range(2) for a, b in zip(CUTS, CUTS[1:])]
    NP = len(W13_PIECES)
    W13_SUM = [4, 6, 7, 8, 7, 8, 9, 13]
    W13_TOTAL = [9, 14]
    W13_ROUND = [9, 10, 11, 11, 15, 17, 17, 17]
    W13_CLIP = [10, 10, 12, 13, 15, 17, 19, 21]
    W13_PUT = [11, 12, 16, 18, 20, 23, 24, 26]
    for steps in (W13_SUM[:NP // 2], W13_SUM[NP // 2:], W13_TOTAL, W13_ROUND, W13_CLIP, W13_PUT, W2_SUM, W2_QUANT):
        assert steps == sorted(steps)
    U_ORDER0 = []
    for n, tile in enumerate(U_ORDER):
        U_ORDER0.append(tile)
        U_ORDER0 += [("w2", t) for s, a, b in W2_PUT if s == n for t in range(a, b)]
    N_W13 = 2 * HC

    ctx = ExitStack()
    with ctx:
        def sb(name, shape, dt=fp32):
            return ctx.enter_context(nc.sbuf_tensor(name, shape, dt))

        def sem(name):
            return ctx.enter_context(nc.semaphore(name))

        x_in = [sb(f"x_in{k}", [S, D]) for k in range(GB)]
        c_in = [sb(f"c_in{i}", [P, MC, D]) for i in range(2)]
        mask_in = [sb(f"mask_in{p}", [S, GB * M], u8) for p in range(2)]
        bias = [sb(f"bias{i}", [S, M]) for i in range(2)]
        xh1 = [sb(f"xh1_{i}", [S, D]) for i in range(2)]
        xT1 = [sb(f"xT1_{part}", [P, DC, S], fp32r) for part in ("hi", "lo")]
        cT = [sb(f"cT_{part}", [P, DC, MP], fp32r) for part in ("hi", "lo")]
        cn = [sb(f"cn_{part}", [P, MC, D], fp32r) for part in ("hi", "lo")]
        probT = [sb(f"probT_{part}", [P, MC, S], fp32r) for part in ("hi", "lo")]
        score = [sb(f"score_{i}", [S, M]) for i in range(2)]
        prob = [sb(f"prob_{i}", [S, MC * P]) for i in range(2)]
        xh2 = [sb(f"xh2_{i}", [S, D]) for i in range(2)]
        x1 = [[sb(f"x1_{p}{k}", [S, D]) for k in range(GB)] for p in range(2)]
        x2hi = [sb(f"x2hi{p}", [P, DC, NT], fp16) for p in range(2)]
        x2lo = [sb(f"x2lo{p}", [P, DC, NT], fp16) for p in range(2)]
        st1 = [sb(f"st1_{i}", [S, 6]) for i in range(2)]
        mv1 = [sb(f"mv1_{i}", [S, 2]) for i in range(2)]
        rs1 = [sb(f"rs1_{i}", [S, 1]) for i in range(2)]
        st2 = [sb(f"st2_{i}", [S, 6]) for i in range(2)]
        mv2 = [sb(f"mv2_{i}", [S, 2]) for i in range(2)]
        rs2 = [sb(f"rs2_{i}", [S, 1]) for i in range(2)]
        smax = [sb(f"smax_{i}", [S, 1]) for i in range(2)]
        nmax = [sb(f"nmax_{i}", [S, 1]) for i in range(2)]
        gate = [sb(f"gate_{i}", [S, 1]) for i in range(2)]
        rsum = [sb(f"rsum_{i}", [S, 1]) for i in range(2)]
        rinv = [sb(f"rinv_{i}", [S, 1]) for i in range(2)]
        alpha = [sb(f"alpha_{i}", [S, 1]) for i in range(2)]
        region = [sb("region0", [P, HC * D]), sb("region1", [P, max(6 * NT + DC * NT + GB * D, HC * D)])]
        wraw = [region[i][:, 0:HC * D] for i in range(2)]
        parts = region[0][:, 0:HC * NT].bitcast(fp16).rearrange("p (a c t) -> p a c t", a=2, t=NT)
        ghi, glo = parts[:, 0, :, :], parts[:, 1, :, :]
        work = region[1]
        th, au, gf = [[work[:, (2 * n + i) * NT:(2 * n + i + 1) * NT] for i in range(2)] for n in range(3)]
        yT = work[:, 6 * NT:(6 + DC) * NT].rearrange("p (c t) -> p c t", t=NT)
        fin = [work[0:S, (6 + DC) * NT + k * D:(6 + DC) * NT + (k + 1) * D] for k in range(GB)]
        w2raw = [sb(f"w2raw{i}", [P, HP]) for i in range(2)]
        w1T = sb("w1T", [P, DC, HP], fp16)
        w3T = sb("w3T", [P, DC, HP], fp16)
        w2T = sb("w2T", [P, HC, D], fp16)
        asum = sb("asum", [P, HC + NP // 2 + DC])
        magic = sb("magic", [P, 2])
        inv = sb("inv", [P, 3])
        tot = sb("tot", [P, 3])
        half = sb("half", [P, 3])
        ident = sb("ident", [P, P])
        ones = sb("ones", [P, P])
        power = sb("power", [P, 1])
        gates = sb("gates", [P, 2])
        tgates = sb("tgates", [P, 2])
        c_tanh = sb("c_tanh", [P, 1])
        beta = sb("beta", [P, 1])
        btmp = sb("btmp", [P, 2])

        def bank(name):
            return ctx.enter_context(nc.psum_tensor(name, [P, 512], fp32))

        Tb = [bank(f"Tb{i}") for i in range(NTB)]
        Sb = bank("Sb")
        Rb = bank("Rb")
        Ub = [bank(f"Ub{i}") for i in range(NUB)]

        x_loaded = [sem(f"x_loaded{k}") for k in range(GB)]
        c_loaded = [sem(f"c_loaded{i}") for i in range(2)]
        mask_loaded = [sem(f"mask_loaded{p}") for p in range(2)]
        w_loaded = [sem(f"w_loaded{p}") for p in range(NP)]
        w2_loaded = [sem(f"w2_loaded{i}") for i in range(2)]
        gates_loaded = sem("gates_loaded")
        stored = [sem(f"stored{k}") for k in range(GB)]
        cpad_ready = sem("cpad_ready")
        consts_ready = sem("consts_ready")
        wpad_ready = sem("wpad_ready")
        setup_done = sem("setup_done")
        setup_chain = sem("setup_chain")
        tanh_ready = sem("tanh_ready")
        asum_ready = sem("asum_ready")
        asum3_ready = sem("asum3_ready")
        tot_ready = sem("tot_ready")
        tot_read = sem("tot_read")
        inv_ready = sem("inv_ready")
        rounded = sem("rounded")
        wq_ready = sem("wq_ready")
        wt_ready = sem("wt_ready")
        wt_act = sem("wt_act")
        wt_dve = sem("wt_dve")
        coef_ready = sem("coef_ready")
        bias_ready = sem("bias_ready")
        stats1 = sem("stats1")
        rstd1 = sem("rstd1")
        xh1_ready = sem("xh1_ready")
        t_ready = sem("t_ready")
        xT1_ready = sem("xT1_ready")
        xT1lo_ready = sem("xT1lo_ready")
        cT_ready = sem("cT_ready")
        cTlo_ready = sem("cTlo_ready")
        cn_ready = sem("cn_ready")
        cnlo_ready = sem("cnlo_ready")
        scores_ready = sem("scores_ready")
        masked_ready = sem("masked_ready")
        nmax_ready = sem("nmax_ready")
        gate_ready = sem("gate_ready")
        prob_ready = sem("prob_ready")
        rinv_ready = sem("rinv_ready")
        alpha_ready = sem("alpha_ready")
        probT_ready = sem("probT_ready")
        probTlo_ready = sem("probTlo_ready")
        readout_ready = sem("readout_ready")
        x1_ready = sem("x1_ready")
        stats2 = sem("stats2")
        rstd2 = sem("rstd2")
        xh2_ready = sem("xh2_ready")
        x2hi_ready = sem("x2hi_ready")
        x2lo_ready = sem("x2lo_ready")
        ln_chain = sem("ln_chain")
        u1_ready = sem("u1_ready")
        u3_ready = sem("u3_ready")
        th_ready = sem("th_ready")
        au_ready = sem("au_ready")
        gf_ready = sem("gf_ready")
        ghi_ready = sem("ghi_ready")
        glo_ready = sem("glo_ready")
        yps_ready = sem("yps_ready")
        yT_ready = sem("yT_ready")
        out_ready = sem("out_ready")
        fin_ready = sem("fin_ready")

        block = ctx.enter_context(nc.Block())

        def sums_of(n):
            start = (0, HC, HC + NP // 2)[n]
            return start, start + (HC, NP // 2, DC)[n]

        def piece_of(p):
            n, a, b = W13_PIECES[p]
            return wraw[n][:, a * D:b * D]

        def piece_arrived(p):
            return w_loaded[p], 32 if W13_PIECES[p][2] == HC else 16

        def nb(G, k):
            return G.g * GB + (k + 1)

        def nh(G, c):
            return G.g * HC + (c + 1)

        def nt(G, pos):
            return G.g * NTT + (pos + 1)

        def t_released(G, k, name):
            if name == "x1T":
                return xT1lo_ready, nb(G, k)
            if name.startswith("cT"):
                return cTlo_ready, (G.g * GB + k) * DC + int(name[2]) + 1
            if name == "PT":
                return probTlo_ready, nb(G, k)
            return x2lo_ready, nb(G, k)

        def wait_alone(eng, *waits):
            values = [v if isinstance(v, int) else eng.to_reg(v) for _, v in waits]
            eng.wait_ge(setup_done, 1)
            for (semaphore, _), value in zip(waits, values):
                eng.wait_ge(semaphore, value)

        def before(G):
            return Group(G.g - 1, 1 - G.parity, None, G.plan)

        def wait_t_bank(eng, G, pos):
            if pos >= NTB:
                eng.wait_ge(*t_released(G, *G.plan.t_order[pos - NTB]))
            elif not G.first:
                eng.wait_ge(*t_released(before(G), *G.plan.t_order[pos - NTB]))

        def u_order(G):
            return U_ORDER0 if G.first else U_ORDER

        def u_released(G, kind, c):
            if kind == "w2":
                t = N_W13 + c
                return (wt_act if t % 2 == 0 else wt_dve), t // 2 + 1
            if kind == "u1":
                return au_ready, nh(G, c)
            if kind == "u3":
                return gf_ready, nh(G, c)
            if kind == "yT":
                return yT_ready, G.g * DC + (c + 1)
            return fin_ready, nb(G, c)

        def wait_u_bank(eng, G, pos):
            if pos >= NUB:
                eng.wait_ge(*u_released(G, *u_order(G)[pos - NUB]))
            elif not G.first:
                eng.wait_ge(*u_released(before(G), *U_ORDER[pos - NUB]))

        def wait_put(eng, n_tiles):
            eng.wait_ge(wt_act, (n_tiles + 1) // 2)
            if n_tiles >= 2:
                eng.wait_ge(wt_dve, n_tiles // 2)

        def t_bank(G, k, name):
            return Tb[G.plan.t_order.index((k, name)) % NTB]

        def u_bank(G, kind, c):
            return Ub[(u_order(G).index((kind, c)) + len(U_ORDER) * G.parity) % NUB]

        def put_tiles(eng, first, end, engine_parity):
            for t in range(first, end):
                if t % 2 != engine_parity:
                    continue
                eng.wait_ge(wt_ready, t + 1)
                if t < N_W13:
                    n, c = t // HC, t % HC
                    src = Ub[t % NUB][:, 0:DC * P].rearrange("p (c h) -> p c h", h=P)
                    dst = (w1T, w3T)[n][:, :, c * P:(c + 1) * P]
                else:
                    d, q = W2_TILES[t - N_W13]
                    h = min(HC - q * HQ, HQ)
                    src = u_bank(static_group(0), "w2", t - N_W13)[:, 0:h * P].rearrange("p (c h) -> p c h", h=P)
                    dst = w2T[:, q * HQ:q * HQ + h, d * P:(d + 1) * P]
                if engine_parity == 0:
                    eng.activation(dst, src, ACT.Identity, bias=magic[:, 1:2]).then_inc(wt_act, 1)
                else:
                    eng.tensor_scalar(dst, src, MAGIC, None, ALU.subtract).then_inc(wt_dve, 1)

        @block.sync
        def _(sp):
            def load_x(G, k):
                b = G.g * GB + k
                if not G.first:
                    sp.wait_ge(x1_ready, nb(G, k) - GB)
                sp.dma_start(x_in[k][:, :], x[bass.ds(b, 1), :, :].rearrange("a s d -> (a s) d"))\
                    .then_inc(x_loaded[k], 16)

            def load_context(G, k):
                i, b = k % 2, G.g * GB + k
                if k >= 2 or not G.first:
                    wait_alone(sp, (cnlo_ready, nb(G, k) - 2), (cT_ready, (nb(G, k) - 2) * DC))
                src = ctx_in[bass.ds(b, 1), :, :].rearrange("a m d -> (a m) d")
                sp.dma_start(c_in[i][:, 0:MC - 1, :],
                             src[0:(MC - 1) * P, :].rearrange("(c p) d -> p c d", p=P)).then_inc(c_loaded[i], 16)
                sp.dma_start(c_in[i][0:MR, MC - 1, :], src[(MC - 1) * P:M, :]).then_inc(c_loaded[i], 16)

            def load_mask(G):
                b = G.g * GB
                rows = mask[bass.ds(b, GB), :].rearrange("(a b) m -> a (b m)", a=1)
                sp.dma_start(mask_in[G.parity][:, :], rows.broadcast_to([S, GB * M]))\
                    .then_inc(mask_loaded[G.parity], 16)

            def store_batch(G, k):
                b = G.g * GB + k
                sp.wait_ge(fin_ready, nb(G, k))
                sp.dma_start(out[bass.ds(b, 1), :, :].rearrange("a s d -> (a s) d"), fin[k]).then_inc(stored[k], 16)

            first = static_group(0)

            def load_w13(n):
                dst = wraw[n].rearrange("p (c d) -> p c d", d=D)
                w = (w1, w3)[n]
                for p, (m, a, b) in enumerate(W13_PIECES):
                    if m != n:
                        continue
                    full = min(b, HC - 1)
                    sp.dma_start(dst[:, a:full, :], w[a * P:full * P, :].rearrange("(c p) d -> p c d", p=P))\
                        .then_inc(w_loaded[p], 16)
                    if full < b:
                        sp.wait_ge(wpad_ready, n + 1)
                        sp.dma_start(dst[0:HR, HC - 1, :], w[(HC - 1) * P:H, :]).then_inc(w_loaded[p], 16)

            load_x(first, 0)
            load_mask(first)
            for n, g in enumerate((g_xattn, g_ffn)):
                sp.dma_start(gates[:, n:n + 1], g.rearrange("(a b) -> a b", a=1).broadcast_to([P, 1]))\
                    .then_inc(gates_loaded, 16)
            sp.wait_ge(cpad_ready, 2)
            load_context(first, 0)
            load_w13(0)
            load_x(first, 1)
            load_context(first, 1)
            load_w13(1)
            load_x(first, 2)
            load_x(first, 3)

            def load_w2(n):
                if n < 2:
                    sp.wait_ge(wpad_ready, 3 + n)
                elif n < 2 + DC:
                    sp.wait_ge(asum_ready, NP // 2 + n - 1)
                else:
                    sp.wait_ge(wt_ready, N_W13 + (n - DC - 1) * (len(W2_TILES) // DC))
                d = n % DC
                sp.dma_start(w2raw[n % 2][:, 0:H], w2[d * P:(d + 1) * P, :]).then_inc(w2_loaded[n % 2], 16)

            def stretch(F, A, last=False):
                if A is not None:
                    nxt = Group(A.g + 1, 1 - A.parity, None, None)
                    if not last:
                        if not A.first:
                            sp.wait_ge(bias_ready, A.g * GB)
                        load_mask(nxt)
                    for k in range(GB):
                        if F is not None and F.first and k == 2:
                            load_w2(DC + 3)
                        if k < 2:
                            load_context(A, k + 2)
                        elif not last:
                            load_context(nxt, k - 2)
                        if F is not None and F.first and k == 1:
                            load_w2(DC + 2)
                        if not last:
                            load_x(nxt, k)
                if F is not None:
                    for k in range(GB):
                        store_batch(F, k)

            stretch(None, static_group(0))
            for n in range(DC + 2):
                load_w2(n)
            stretch(static_group(0), static_group(1))
            with nc.Fori(0, (NG - 2) // 2 - 1, engines=[sp.engine], hint_back_edge=True) as j:
                pair_of_stretches(stretch, j)
            stretch(static_group(NG - 3), static_group(NG - 2))
            stretch(static_group(NG - 2), static_group(NG - 1), last=True)
            stretch(static_group(NG - 1), None)
            for k in range(GB):
                sp.wait_ge(stored[k], 16 * NG)

        @block.gpsimd
        def _(pool):
            for i in range(2):
                pool.memset(c_in[i][:, MC - 1, :], 0.0).then_inc(cpad_ready, 1)
            pool.memset(ident[:, :], 0.0).then_inc(setup_done, 1)
            pool.wait_ge(setup_done, 1)
            pool.affine_select(out=ident[:, :], in_=ident[:, :], compare_op=ALU.not_equal, fill=1.0, base=0,
                               pattern=[[-1, P]], channel_multiplier=1).then_inc(consts_ready, 1)
            pool.memset(power[:, :], -0.5).then_inc(consts_ready, 1)
            pool.memset(ones[:, :], 1.0).then_inc(consts_ready, 1)
            pool.memset(magic[:, 0:1], MAGIC).then_inc(consts_ready, 1)
            pool.memset(magic[:, 1:2], -MAGIC).then_inc(consts_ready, 1)
            for i in range(2):
                pool.memset(prob[i][:, M:MC * P], 0.0).then_inc(consts_ready, 1)
                pool.memset(cT[i][:, :, M:MP].bitcast(fp32), 0.0).then_inc(consts_ready, 1)
            for n in range(2):
                pool.memset(wraw[n][:, (HC - 1) * D:HC * D], 0.0).then_inc(wpad_ready, 1)
            for i in range(2):
                pool.memset(w2raw[i][:, H:HP], 0.0).then_inc(wpad_ready, 1)
            pool.wait_ge(consts_ready, N_CONSTS)

            def bias_of(G, k):
                used = [(masked_ready, nb(G, k) - 2)] if k >= 2 or not G.first else []
                wait_alone(pool, (mask_loaded[G.parity], (G.half + 1) * 16), *used)
                pool.tensor_scalar(bias[k % 2][:, :], mask_in[G.parity][:, k * M:(k + 1) * M], -NEG, NEG,
                                   ALU.mult, ALU.add).then_inc(bias_ready, 1)

            def low_part(G, c):
                pool.wait_ge(ghi_ready, nh(G, c))
                pool.tensor_tensor(glo[:, c, :], gf[c % 2], ghi[:, c, :], ALU.subtract).then_inc(glo_ready, 1)

            def context_low(G, k):
                pool.wait_ge(cn_ready, nb(G, k))
                pool.tensor_tensor(cn[1][:, :, :], c_in[k % 2][:, :, :], cn[0][:, :, :].bitcast(fp32), ALU.subtract)\
                    .then_inc(cnlo_ready, 1)

            def rstd(G, k, which):
                i = k % 2
                mv, rs = (mv1, rs1) if which == 1 else (mv2, rs2)
                pool.wait_ge(stats1 if which == 1 else stats2, nb(G, k))
                pool.tensor_tensor(rs[i][:, 0:1], mv[i][:, 1:2], power[0:S, :], ALU.pow)\
                    .then_inc(rstd1 if which == 1 else rstd2, 1)

            def stretch(F, A):
                for s in range(A.plan.slots if F is None else SLOTS):
                    if F is not None and 3 <= s <= HSLOTS + 1 and s % 2 == 1:
                        low_part(F, s // 2 - 1)
                    if A is not None:
                        for k, name in A.plan.at(s, OTHER_STEPS):
                            if name == "stats1":
                                rstd(A, k, 1)
                                bias_of(A, k)
                            if name == "split":
                                context_low(A, k)
                            if name == "res1":
                                rstd(A, k, 2)

            stretch(None, static_group(0))
            stretch(static_group(0), static_group(1))
            with nc.Fori(0, (NG - 2) // 2, engines=[pool.engine], hint_back_edge=True) as j:
                pair_of_stretches(stretch, j)
            stretch(static_group(NG - 1), None)

        @block.scalar
        def _(act):
            act.wait_ge(gates_loaded, 32)
            act.activation(tgates[:, :], gates[:, :], ACT.Tanh).then_inc(tanh_ready, 1)

            def read_t(G, k, name):
                src = t_bank(G, k, name)
                if (k, name) == next(step for step in G.plan.t_order if step[0] == k) and (k or not G.first):
                    act.wait_ge(scores_ready, nb(G, k) - 1)
                act.wait_ge(t_ready, nt(G, G.plan.t_order.index((k, name))))
                if name == "x1T":
                    act.activation(xT1[0][:, :, :], src[:, 0:DC * S].rearrange("p (c s) -> p c s", s=S), ACT.Copy)\
                        .then_inc(xT1_ready, 1)
                elif name.startswith("cT"):
                    act.activation(cT[0][:, int(name[2]), 0:M], src[:, 0:M], ACT.Copy).then_inc(cT_ready, 1)
                elif name == "PT":
                    act.activation(probT[0][:, :, :], src[:, 0:MC * S].rearrange("p (c s) -> p c s", s=S), ACT.Copy)\
                        .then_inc(probT_ready, 1)
                else:
                    act.activation(x2hi[G.parity][:, :, k * S:(k + 1) * S],
                                   src[:, 0:DC * S].rearrange("p (c s) -> p c s", s=S), ACT.Copy, scale=XS)\
                        .then_inc(x2hi_ready, 1)

            def context_high(G, k):
                act.wait_ge(c_loaded[k % 2], (G.g * (GB // 2) + k // 2 + 1) * 32)
                if k or not G.first:
                    act.wait_ge(readout_ready, nb(G, k) - 1)
                act.activation(cn[0][:, :, :], c_in[k % 2][:, :, :], ACT.Copy).then_inc(cn_ready, 1)

            def softmax_exp(G, k):
                i = k % 2
                act.wait_ge(nmax_ready, nb(G, k))
                act.activation(prob[i][:, 0:M], score[i][:, :], ACT.Exp, bias=nmax[i][:, :], scale=SCALE,
                               accum_out=rsum[i][:, :]).then_inc(prob_ready, 1)

            def gate_tanh(G, c):
                act.wait_ge(u1_ready, nh(G, c))
                act.activation(th[c % 2], u_bank(G, "u1", c)[:, 0:NT], ACT.Tanh, scale=c_tanh[:, :])\
                    .then_inc(th_ready, 1)

            def high_part(G, c):
                act.wait_ge(gf_ready, nh(G, c))
                act.activation(ghi[:, c, :], gf[c % 2], ACT.Copy).then_inc(ghi_ready, 1)

            def read_y(G, c):
                act.wait_ge(yps_ready, G.g * DC + (c + 1))
                act.activation(yT[:, c, :], u_bank(G, "yT", c)[:, 0:NT], ACT.Copy).then_inc(yT_ready, 1)

            def sum_w3(p):
                act.wait_ge(*piece_arrived(p))
                _, a, b = W13_PIECES[p]
                column = sums_of(1)[0] + p - NP // 2
                act.activation(w3T[:, :, :].rearrange("p c h -> p (c h)")[:, a * D:b * D], piece_of(p), ACT.Abs,
                               accum_out=asum[:, column:column + 1]).then_inc(asum3_ready, 1)

            def round_weights(n, raw, loaded, value):
                act.wait_ge(inv_ready, n + 1)
                act.wait_ge(loaded, value)
                act.activation(raw, raw, ACT.Identity, scale=inv[:, n:n + 1], bias=magic[:, 0:1]).then_inc(rounded, 1)

            def weights(F, A, s):
                if F is None and A.first:
                    for p, (n, a, b) in enumerate(W13_PIECES):
                        if s == W13_SUM[p] and n == 1:
                            sum_w3(p)
                        if s == W13_ROUND[p]:
                            round_weights(n, piece_of(p), *piece_arrived(p))
                        if s == W13_PUT[p]:
                            put_tiles(act, n * HC + a, n * HC + b, 0)
                if F is not None and F.first:
                    for d in range(DC):
                        if s == W2_QUANT[d]:
                            round_weights(2, w2raw[d % 2][:, :], w2_loaded[d % 2], (d // 2 + 3) * 16)
                    for at, a, b in W2_PUT:
                        if s == at + 1:
                            put_tiles(act, N_W13 + a, N_W13 + b, 0)

            def stretch(F, A):
                for s in range(A.plan.slots if F is None else SLOTS):
                    if F is not None and s < HSLOTS and s % 2 == 1:
                        gate_tanh(F, s // 2)
                    if A is not None:
                        for k, name in A.plan.at(s, T_STEPS):
                            read_t(A, k, name)
                        for k, name in A.plan.at(s, OTHER_STEPS):
                            if name == "split":
                                context_high(A, k)
                            if name == "exp":
                                softmax_exp(A, k)
                    weights(F, A, s)
                    if F is not None:
                        if 2 <= s <= HSLOTS and s % 2 == 0:
                            high_part(F, s // 2 - 1)
                        if s > HSLOTS and (s - HSLOTS) % 2 == 0:
                            read_y(F, (s - HSLOTS) // 2 - 1)
                if F is not None:
                    read_y(F, DC - 1)

            act.wait_ge(consts_ready, N_CONSTS)
            stretch(None, static_group(0))
            act.wait_ge(coef_ready, 1)
            stretch(static_group(0), static_group(1))
            with nc.Fori(0, (NG - 2) // 2, engines=[act.engine], hint_back_edge=True) as j:
                pair_of_stretches(stretch, j)
            stretch(static_group(NG - 1), None)

        @block.vector
        def _(dve):
            chained = [0]

            def link(ins):
                chained[0] += 1
                ins.then_inc(setup_chain, 1)
                dve.wait_ge(setup_chain, chained[0])

            ln_count = [0]

            def stats(G, k, which):
                i = k % 2
                at = G.g * (4 * GB) + ln_count[0] % (4 * GB)
                ln_count[0] += 2
                src, st, mv = (x_in[k], st1[i], mv1[i]) if which == 1 else (x1[G.parity][k], st2[i], mv2[i])
                if which == 1:
                    dve.wait_ge(x_loaded[k], (G.g + 1) * 16)
                else:
                    dve.wait_ge(x1_ready, nb(G, k))
                dve.bn_stats(st[:, :], src[:, :]).then_inc(ln_chain, 1)
                wait_alone(dve, (ln_chain, at + 1))
                dve.bn_aggr(mv[:, :], st[:, :]).then_inc(ln_chain, 1)
                dve.wait_ge(ln_chain, at + 2)
                dve.tensor_scalar(mv[:, 1:2], mv[:, 1:2], EPS, None, ALU.add)\
                    .then_inc(stats1 if which == 1 else stats2, 1)

            def normalise(G, k, which):
                i = k % 2
                if which == 1:
                    src, mv, rs, dst, ready, done = x_in[k], mv1[i], rs1[i], xh1[i], rstd1, xh1_ready
                else:
                    src, mv, rs, dst, ready, done = x1[G.parity][k], mv2[i], rs2[i], xh2[i], rstd2, xh2_ready
                dve.wait_ge(ready, nb(G, k))
                dve.tensor_scalar(dst[:, :], src[:, :], mv[:, 0:1], rs[:, 0:1], ALU.subtract, ALU.mult)\
                    .then_inc(done, 1)

            def masked_max(G, k):
                i = k % 2
                wait_alone(dve, (scores_ready, nb(G, k)), (bias_ready, nb(G, k)))
                dve.tensor_tensor_reduce(out=score[i][:, :], in0=Sb[0:S, 0:M], in1=bias[i][:, :], scale=1.0, scalar=-3e38,
                                         op0=ALU.add, op1=ALU.max, accum_out=smax[i][:, :]).then_inc(masked_ready, 1)
                dve.wait_ge(masked_ready, nb(G, k))
                dve.tensor_scalar(nmax[i][:, :], smax[i][:, :], -SCALE, None, ALU.mult).then_inc(nmax_ready, 1)
                if G.first and k == 0:
                    dve.wait_ge(tanh_ready, 1)
                dve.tensor_scalar(gate[i][:, :], smax[i][:, :], 0.5 * NEG, tgates[0:S, 0:1], ALU.is_gt, ALU.mult)\
                    .then_inc(gate_ready, 1)

            def first_residual(G, k):
                i = k % 2
                dve.wait_ge(prob_ready, nb(G, k))
                dve.reciprocal(rinv[i][:, :], rsum[i][:, :]).then_inc(rinv_ready, 1)
                dve.wait_ge(rinv_ready, nb(G, k))
                dve.wait_ge(gate_ready, nb(G, k))
                dve.tensor_tensor(alpha[i][:, :], rinv[i][:, :], gate[i][:, :], ALU.mult).then_inc(alpha_ready, 1)
                dve.wait_ge(alpha_ready, nb(G, k))
                dve.wait_ge(readout_ready, nb(G, k))
                dve.scalar_tensor_tensor(x1[G.parity][k][:, :], Rb[0:S, :], alpha[i][:, :], x_in[k][:, :],
                                         ALU.mult, ALU.add).then_inc(x1_ready, 1)

            def x2_low(G, k):
                dve.wait_ge(x2hi_ready, nb(G, k))
                dve.scalar_tensor_tensor(x2lo[G.parity][:, :, k * S:(k + 1) * S],
                                         t_bank(G, k, "x2T")[:, 0:DC * S].rearrange("p (c s) -> p c s", s=S), XS,
                                         x2hi[G.parity][:, :, k * S:(k + 1) * S], ALU.mult, ALU.subtract)\
                    .then_inc(x2lo_ready, 1)

            def low(G, k, name):
                src = t_bank(G, k, name)
                if name == "x1T":
                    dve.wait_ge(xT1_ready, nb(G, k))
                    dve.tensor_tensor(xT1[1][:, :, :], src[:, 0:DC * S].rearrange("p (c s) -> p c s", s=S),
                                      xT1[0][:, :, :].bitcast(fp32), ALU.subtract).then_inc(xT1lo_ready, 1)
                elif name.startswith("cT"):
                    d = int(name[2])
                    dve.wait_ge(cT_ready, (G.g * GB + k) * DC + d + 1)
                    dve.tensor_tensor(cT[1][:, d, 0:M], src[:, 0:M], cT[0][:, d, 0:M].bitcast(fp32), ALU.subtract)\
                        .then_inc(cTlo_ready, 1)
                elif name == "PT":
                    dve.wait_ge(probT_ready, nb(G, k))
                    dve.tensor_tensor(probT[1][:, :, :], src[:, 0:MC * S].rearrange("p (c s) -> p c s", s=S),
                                      probT[0][:, :, :].bitcast(fp32), ALU.subtract).then_inc(probTlo_ready, 1)

            def silu_part(G, c):
                dve.wait_ge(th_ready, nh(G, c))
                dve.scalar_tensor_tensor(au[c % 2], th[c % 2], 1.0, u_bank(G, "u1", c)[:, 0:NT],
                                         ALU.add, ALU.mult).then_inc(au_ready, 1)

            def gated(G, c):
                dve.wait_ge(au_ready, nh(G, c))
                dve.wait_ge(u3_ready, nh(G, c))
                if c >= 2:
                    dve.wait_ge(glo_ready, nh(G, c) - 2)
                dve.scalar_tensor_tensor(gf[c % 2], au[c % 2], GS / (2 * XS * XS),
                                         u_bank(G, "u3", c)[:, 0:NT], ALU.mult, ALU.mult).then_inc(gf_ready, 1)

            def second_residual(G, k):
                dve.wait_ge(out_ready, nb(G, k))
                if not G.first:
                    dve.wait_ge(stored[k], G.g * 16)
                dve.scalar_tensor_tensor(fin[k], u_bank(G, "out", k)[0:S, :], beta[0:S, :],
                                         x1[G.parity][k][:, :], ALU.mult, ALU.add).then_inc(fin_ready, 1)

            def mean_of(n):
                dve.wait_ge(tot_ready, n + 1)
                a, b = sums_of(n)
                dve.tensor_reduce(tot[:, n:n + 1], Sb[:, MP:MP + b - a], AX.X, ALU.add).then_inc(tot_read, 1)
                dve.wait_ge(tot_read, n + 1)
                link(dve.reciprocal(half[:, n:n + 1], tot[:, n:n + 1]))
                dve.tensor_scalar(inv[:, n:n + 1], half[:, n:n + 1], N_W, None, ALU.mult).then_inc(inv_ready, 1)
                dve.wait_ge(inv_ready, n + 1)
                link(dve.tensor_scalar(half[:, n:n + 1], tot[:, n:n + 1], 1.0 / N_W, 0.5, ALU.mult, ALU.mult))
                if n == 0:
                    dve.tensor_scalar(c_tanh[:, :], half[:, 0:1], 1.0 / XS, None, ALU.mult).then_inc(coef_ready, 1)
                if n == 2:
                    link(dve.tensor_tensor(btmp[:, 0:1], half[:, 0:1], half[:, 1:2], ALU.mult))
                    link(dve.tensor_tensor(btmp[:, 1:2], btmp[:, 0:1], half[:, 2:3], ALU.mult))
                    link(dve.tensor_scalar(beta[:, :], btmp[:, 1:2], tgates[:, 1:2], 8.0 / GS, ALU.mult, ALU.mult))

            def clip(n, raw):
                dve.wait_ge(rounded, n + 1)
                dve.tensor_scalar(raw, raw, MAGIC + 1.0, MAGIC - 1.0, ALU.min, ALU.max).then_inc(wq_ready, 1)

            def weights(F, A, s):
                if F is None and A.first:
                    for p, (n, a, b) in enumerate(W13_PIECES):
                        if s == W13_SUM[p] and n == 0:
                            dve.wait_ge(*piece_arrived(p))
                            dve.tensor_reduce(asum[:, a:b], piece_of(p).rearrange("p (c d) -> p c d", d=D),
                                              AX.X, ALU.add, apply_absolute_value=True).then_inc(asum_ready, 1)
                        if s == W13_CLIP[p]:
                            clip(p, piece_of(p))
                        if s == W13_PUT[p]:
                            put_tiles(dve, n * HC + a, n * HC + b, 1)
                    for n in range(2):
                        if s == W13_TOTAL[n]:
                            mean_of(n)
                if F is not None and F.first:
                    for d in range(DC):
                        if s == W2_SUM[d]:
                            dve.wait_ge(w2_loaded[d % 2], (d // 2 + 1) * 16)
                            column = sums_of(2)[0] + d
                            dve.tensor_reduce(asum[:, column:column + 1], w2raw[d % 2][:, :], AX.X, ALU.add,
                                              apply_absolute_value=True).then_inc(asum_ready, 1)
                        if s == W2_QUANT[d] + 1:
                            clip(NP + d, w2raw[d % 2][:, :])
                    if s == W2_TOTALS[0]:
                        mean_of(2)
                    for at, a, b in W2_PUT:
                        if s == at + 1:
                            put_tiles(dve, N_W13 + a, N_W13 + b, 1)

            def stretch(F, A):
                for s in range(A.plan.slots if F is None else SLOTS):
                    if F is not None and s < HSLOTS and s % 2 == 1:
                        silu_part(F, s // 2)
                    if F is not None and 2 <= s <= HSLOTS and s % 2 == 0:
                        gated(F, s // 2 - 1)
                    if A is not None:
                        for k, name in A.plan.at(s, T_STEPS):
                            if name == "x2T":
                                x2_low(A, k)
                            else:
                                low(A, k, name)
                        for k, name in A.plan.at(s, OTHER_STEPS):
                            if name == "stats1":
                                stats(A, k, 1)
                            if name == "norm1":
                                normalise(A, k, 1)
                            if name == "max":
                                masked_max(A, k)
                            if name == "res1":
                                first_residual(A, k)
                                stats(A, k, 2)
                            if name == "norm2":
                                normalise(A, k, 2)
                    weights(F, A, s)
                if F is not None:
                    for k in range(GB):
                        second_residual(F, k)

            dve.wait_ge(consts_ready, N_CONSTS)
            stretch(None, static_group(0))
            stretch(static_group(0), static_group(1))
            with nc.Fori(0, (NG - 2) // 2, engines=[dve.engine], hint_back_edge=True) as j:
                pair_of_stretches(stretch, j)
            stretch(static_group(NG - 1), None)

        @block.tensor
        def _(pe):
            mrows = [P] * (MC - 1) + [MR]
            PRODUCTS = [(0, 0), (0, 1), (1, 0)]

            def totals(G, k):
                at, prev = G.plan.slot[k, "scores"], G.plan.slot[k - 1, "scores"] if k else -1
                if isinstance(G.g, int) and G.g == 0:
                    return [n + 1 for n in range(2) if prev <= W13_TOTAL[n] < at]
                if isinstance(G.g, int) and G.g == 1:
                    return [3] if prev <= W2_TOTALS[0] < at else []
                return []

            def total(n, scored):
                if n == 1:
                    pe.wait_ge(asum3_ready, NP // 2)
                else:
                    pe.wait_ge(asum_ready, NP // 2 if n == 0 else NP // 2 + DC)
                pe.wait_ge(masked_ready, scored)
                a, b = sums_of(n)
                pe.matmul(Sb[:, MP:MP + b - a], ones[:, :], asum[:, a:b], start=True, stop=True)\
                    .then_inc(tot_ready, 1)

            def transpose_weights(bank, pieces):
                for j, piece in enumerate(pieces):
                    last = pe.transpose(bank[:, j * P:(j + 1) * P], piece, ident[:, :])
                last.then_inc(wt_ready, 1)

            def weights(F, A, s):
                if F is None and A.first:
                    for n in range(2):
                        if s == W13_TOTAL[n]:
                            total(n, sum(A.plan.slot[k, "scores"] <= s for k in range(GB)))
                    for p, (n, a, b) in enumerate(W13_PIECES):
                        if s == W13_PUT[p]:
                            pe.wait_ge(wq_ready, p + 1)
                            for t in range(n * HC + a, n * HC + b):
                                if t >= NUB:
                                    wait_put(pe, t - NUB + 1)
                                c = t % HC
                                transpose_weights(Ub[t % NUB], [wraw[n][:, c * D + d * P:c * D + (d + 1) * P]
                                                                for d in range(DC)])
                if F is not None and F.first:
                    if s == W2_TOTALS[0]:
                        total(2, GB + sum(A.plan.slot[k, "scores"] <= s for k in range(GB)))
                    for at, a, b in W2_PUT:
                        if s != at:
                            continue
                        for t in range(a, b):
                            d, q = W2_TILES[t]
                            pe.wait_ge(wq_ready, NP + d + 1)
                            wait_u_bank(pe, F, U_ORDER0.index(("w2", t)))
                            transpose_weights(u_bank(F, "w2", t), [w2raw[d % 2][:, c * P:(c + 1) * P]
                                                                   for c in range(q * HQ, min(HC, (q + 1) * HQ))])

            def attention_step(G, k, name):
                i = k % 2
                if name in T_STEPS:
                    pos = G.plan.t_order.index((k, name))
                    dst = t_bank(G, k, name)
                    wait_t_bank(pe, G, pos)
                if name == "x1T":
                    pe.wait_ge(xh1_ready, nb(G, k))
                    for c in range(DC):
                        last = pe.transpose(dst[:, c * S:(c + 1) * S], xh1[i][:, c * P:(c + 1) * P], ident[0:S, 0:S])
                    last.then_inc(t_ready, 1)
                elif name.startswith("cT"):
                    d = int(name[2])
                    if d == 0:
                        pe.wait_ge(c_loaded[i], (G.g * (GB // 2) + k // 2 + 1) * 32)
                    for m, rows in enumerate(mrows):
                        last = pe.transpose(dst[:, m * P:m * P + rows], c_in[i][0:rows, m, d * P:(d + 1) * P],
                                            ident[0:rows, 0:rows])
                    last.then_inc(t_ready, 1)
                elif name == "scores":
                    pe.wait_ge(xT1lo_ready, nb(G, k))
                    pe.wait_ge(cTlo_ready, nb(G, k) * DC)
                    if k or not G.first:
                        pe.wait_ge(masked_ready, nb(G, k) - 1)
                    for n in totals(G, k):
                        pe.wait_ge(tot_read, n)
                    terms = [(c, a, b) for c in range(DC) for a, b in PRODUCTS]
                    for c, a, b in terms:
                        last = pe.matmul(Sb[0:S, 0:MP], xT1[a][:, c, :], cT[b][:, c, :],
                                         start=(c, a, b) == terms[0], stop=(c, a, b) == terms[-1])
                    last.then_inc(scores_ready, 1)
                elif name == "PT":
                    pe.wait_ge(prob_ready, nb(G, k))
                    for m in range(MC):
                        last = pe.transpose(dst[:, m * S:(m + 1) * S], prob[i][:, m * P:(m + 1) * P], ident[0:S, 0:S])
                    last.then_inc(t_ready, 1)
                elif name == "readout":
                    pe.wait_ge(probTlo_ready, nb(G, k))
                    pe.wait_ge(cnlo_ready, nb(G, k))
                    if k or not G.first:
                        pe.wait_ge(x1_ready, nb(G, k) - 1)
                    terms = [(m, a, b) for m in range(MC) for a, b in PRODUCTS]
                    for m, a, b in terms:
                        last = pe.matmul(Rb[0:S, :], probT[a][0:mrows[m], m, :], cn[b][0:mrows[m], m, :],
                                         start=(m, a, b) == terms[0], stop=(m, a, b) == terms[-1])
                    last.then_inc(readout_ready, 1)
                else:
                    pe.wait_ge(xh2_ready, nb(G, k))
                    for c in range(DC):
                        last = pe.transpose(dst[:, c * S:(c + 1) * S], xh2[i][:, c * P:(c + 1) * P], ident[0:S, 0:S])
                    last.then_inc(t_ready, 1)

            def project(G, s):
                c, kind = s // 2, ("u1", "u3")[s % 2]
                w, ready = (w1T, u1_ready) if kind == "u1" else (w3T, u3_ready)
                dst = u_bank(G, kind, c)
                wait_u_bank(pe, G, u_order(G).index((kind, c)))
                if s == 0:
                    pe.wait_ge(x2lo_ready, nb(G, GB - 1))
                for d in range(DC):
                    for part in (x2hi, x2lo):
                        last = pe.matmul(dst[:, 0:NT], w[:, d, c * P:(c + 1) * P], part[G.parity][:, d, :],
                                         start=d == 0 and part is x2hi, stop=d == DC - 1 and part is x2lo)
                last.then_inc(ready, 1)

            def down(G, s):
                d, part = (s - HSLOTS) // 2, (s - HSLOTS) % 2
                dst = u_bank(G, "yT", d)
                mid = (HC + 1) // 2
                if G.first and s == HSLOTS:
                    wait_put(pe, N_W13 + len(W2_TILES))
                if part == 0:
                    wait_u_bank(pe, G, u_order(G).index(("yT", d)))
                for c in range(0, mid) if part == 0 else range(mid, HC):
                    if d == 0:
                        pe.wait_ge(glo_ready, nh(G, c))
                    for g in (ghi, glo):
                        last = pe.matmul(dst[:, 0:NT], w2T[:, c, d * P:(d + 1) * P], g[:, c, :],
                                         start=c == 0 and g is ghi, stop=c == HC - 1 and g is glo)
                if part == 1:
                    last.then_inc(yps_ready, 1)

            def outputs(G):
                for pair in range(0, GB, 2):
                    for d in range(DC):
                        if pair == 0:
                            pe.wait_ge(yT_ready, G.g * DC + (d + 1))
                        for k in range(pair, pair + 2):
                            dst = u_bank(G, "out", k)
                            if d == 0:
                                wait_u_bank(pe, G, u_order(G).index(("out", k)))
                            made = pe.transpose(dst[0:S, d * P:(d + 1) * P], yT[:, d, k * S:(k + 1) * S], ident[:, :])
                            if d == DC - 1:
                                made.then_inc(out_ready, 1)

            def stretch(F, A):
                for s in range(A.plan.slots if F is None else SLOTS):
                    if A is not None:
                        for k, name in A.plan.at(s, PE_STEPS):
                            attention_step(A, k, name)
                    if F is not None:
                        if s < HSLOTS:
                            project(F, s)
                        else:
                            down(F, s)
                    weights(F, A, s)
                if F is not None:
                    outputs(F)

            pe.wait_ge(consts_ready, N_CONSTS)
            stretch(None, static_group(0))
            wait_put(pe, N_W13)
            stretch(static_group(0), static_group(1))
            with nc.Fori(0, (NG - 2) // 2, engines=[pe.engine], hint_back_edge=True) as j:
                pair_of_stretches(stretch, j)
            stretch(static_group(NG - 1), None)


_INS = ["x", "ctx_2048", "mask_BxS2_bk0", "g_xattn", "g_ffn", "L0_ffn_w1", "L0_ffn_w3", "L0_ffn_w2"]


def kernel(**inputs):
    import numpy as _np
    import concourse.bacc as _bacc
    from concourse import mybir as _mybir
    from concourse.bass_utils import run_bass_kernel_spmd as _run

    nc = _bacc.Bacc("TRN2", target_bir_lowering=False, num_devices=1)
    arrays, args = {}, []
    for name in _INS:
        a = _np.ascontiguousarray(inputs[name])
        arrays[f"in_{name}_dram"] = a
        args.append(nc.dram_tensor(f"in_{name}_dram", a.shape, _mybir.dt.from_np(a.dtype), kind="ExternalInput").ap())
    shape = inputs["x"].shape
    args.append(nc.dram_tensor("out_0_dram", shape, _mybir.dt.float32, kind="ExternalOutput").ap())
    gated_block(nc, *args)
    r = _run(nc, [arrays], core_ids=[0])
    return r.results[0]["out_0_dram"]
```
